# Optimizing a Trainium2 kernel written in Bass

```python
import numpy as np
import jax
import jax.numpy as jnp

def _softmax(x, axis=-1):
    return jax.nn.softmax(x, axis=axis)

def _gelu(x):
    return jax.nn.gelu(x, approximate=True)

def _silu(x):
    return jax.nn.silu(x)

def _sigmoid(x):
    return jax.nn.sigmoid(x)

def _layernorm(x, axis=-1, eps=1e-05):
    m = jnp.mean(x, axis=axis, keepdims=True)
    v = jnp.var(x, axis=axis, keepdims=True)
    return (x - m) / jnp.sqrt(v + eps)

def _scatter_add(tgt, idx, src, axis=0):
    return tgt.at[idx].add(src)

def _segment_sum(src, seg, n):
    return jax.ops.segment_sum(src, seg, n)
kernel_name = 'mk_sandwich_d1_jaxref_r4_5d108b'

def setup_inputs(seed: int=0):
    np.random.seed(seed)
    _w = jnp.asarray

    def _L0_attn_setup():
        import jax, jax.numpy as jnp
        import numpy as np
        EPS = 0.0001

        def wkv_log_space(w, u, k, v):
            B, T, D = k.shape
            neg_inf = jnp.full((B, D), -jnp.inf, dtype=k.dtype)

            def step(carry, kv_t):
                ln_ap, ln_am, ln_b = carry
                kt, vt = kv_t
                ln_vp = jnp.log(jnp.maximum(vt, 0) + EPS)
                ln_vm = jnp.log(jnp.maximum(-vt, 0) + EPS)
                uk = u + kt
                denom = jnp.logaddexp(uk, ln_b)
                wkv_t = jnp.exp(jnp.logaddexp(uk + ln_vp, ln_ap) - denom) - jnp.exp(jnp.logaddexp(uk + ln_vm, ln_am) - denom)
                ln_ap = jnp.logaddexp(ln_ap - w, kt + ln_vp)
                ln_am = jnp.logaddexp(ln_am - w, kt + ln_vm)
                ln_b = jnp.logaddexp(ln_b - w, kt)
                return ((ln_ap, ln_am, ln_b), wkv_t)
            kT = jnp.swapaxes(k, 0, 1)
            vT = jnp.swapaxes(v, 0, 1)
            _, wkv = jax.lax.scan(step, (neg_inf, neg_inf, neg_inf), (kT, vT))
            return jnp.swapaxes(wkv, 0, 1)
        key = jax.random.key(seed)
        ks = jax.random.split(key, 10)
        B, T, D = (8, 512, 256)
        s = D ** (-0.5)
        return {'x': jax.random.normal(ks[0], (B, T, D), jnp.float32), 'time_decay': jax.random.normal(ks[1], (D,), jnp.float32), 'time_first': jax.random.normal(ks[2], (D,), jnp.float32), 'time_mix_k': jax.random.normal(ks[3], (1, 1, D), jnp.float32), 'time_mix_v': jax.random.normal(ks[4], (1, 1, D), jnp.float32), 'time_mix_r': jax.random.normal(ks[5], (1, 1, D), jnp.float32), 'Wk': jax.random.normal(ks[6], (D, D), jnp.float32) * s, 'Wv': jax.random.normal(ks[7], (D, D), jnp.float32) * s, 'Wr': jax.random.normal(ks[8], (D, D), jnp.float32) * s, 'Wo': jax.random.normal(ks[9], (D, D), jnp.float32) * s}
    _L0_attn_in = _L0_attn_setup()

    def _L0_ffn_setup():
        import jax, jax.numpy as jnp
        import numpy as np
        D = 256
        F = 256
        E = 8
        K = 2
        B, T = (2, 512)

        def _moe_forward(x, router_w, w1, w2, shared_gate_up, shared_down, shared_gate_w):
            b, t, d = x.shape
            xf = x.reshape(-1, d)
            n = xf.shape[0]
            logits = xf @ router_w
            probs = jax.nn.softmax(logits, axis=-1)
            topw, topi = jax.lax.top_k(probs, K)
            combine = jnp.zeros((n, E), dtype=probs.dtype).at[jnp.arange(n)[:, None], topi].add(topw)
            h = jax.nn.silu(jnp.einsum('nd,edf->nef', xf, w1))
            ye = jnp.einsum('nef,efd->ned', h, w2)
            routed = jnp.einsum('ne,ned->nd', combine, ye)
            gu = xf @ shared_gate_up
            gate, up = (gu[:, :F], gu[:, F:])
            shared = jax.nn.silu(gate) * up @ shared_down
            shared = jax.nn.sigmoid(xf @ shared_gate_w) * shared
            return (routed + shared).reshape(b, t, d)
        key = jax.random.key(seed)
        ks = jax.random.split(key, 7)
        std = 0.02
        x = jax.random.normal(ks[0], (B, T, D), dtype=jnp.float32)
        router_w = jax.random.normal(ks[1], (D, E), dtype=jnp.float32) * std
        w1 = jax.random.normal(ks[2], (E, D, F), dtype=jnp.float32) * std
        w2 = jax.random.normal(ks[3], (E, F, D), dtype=jnp.float32) * std
        shared_gate_up = jax.random.normal(ks[4], (D, 2 * F), dtype=jnp.float32) * std
        shared_down = jax.random.normal(ks[5], (F, D), dtype=jnp.float32) * std
        shared_gate_w = jax.random.normal(ks[6], (D, 1), dtype=jnp.float32) * std
        return {'x': x, 'router_w': router_w, 'w1': w1, 'w2': w2, 'shared_gate_up': shared_gate_up, 'shared_down': shared_down, 'shared_gate_w': shared_gate_w}
    _L0_ffn_in = _L0_ffn_setup()
    _d = {'L0_attn_x': _L0_attn_in['x'], 'L0_attn_time_decay': _L0_attn_in['time_decay'], 'L0_attn_time_first': _L0_attn_in['time_first'], 'L0_attn_time_mix_k': _L0_attn_in['time_mix_k'], 'L0_attn_time_mix_v': _L0_attn_in['time_mix_v'], 'L0_attn_time_mix_r': _L0_attn_in['time_mix_r'], 'L0_attn_Wk': _L0_attn_in['Wk'], 'L0_attn_Wv': _L0_attn_in['Wv'], 'L0_attn_Wr': _L0_attn_in['Wr'], 'L0_attn_Wo': _L0_attn_in['Wo'], 'L0_ffn_router_w': _L0_ffn_in['router_w'], 'L0_ffn_w1': _L0_ffn_in['w1'], 'L0_ffn_w2': _L0_ffn_in['w2'], 'L0_ffn_shared_gate_up': _L0_ffn_in['shared_gate_up'], 'L0_ffn_shared_down': _L0_ffn_in['shared_down'], 'L0_ffn_shared_gate_w': _L0_ffn_in['shared_gate_w']}
    _x0 = _d['L0_attn_x']
    _d['L0_attn_x'] = jax.random.normal(jax.random.fold_in(jax.random.key(seed), 1), (8, 2048, 256), dtype=_x0.dtype)
    del _x0
    return _d

def reference(L0_attn_x, L0_attn_time_decay, L0_attn_time_first, L0_attn_time_mix_k, L0_attn_time_mix_v, L0_attn_time_mix_r, L0_attn_Wk, L0_attn_Wv, L0_attn_Wr, L0_attn_Wo, L0_ffn_router_w, L0_ffn_w1, L0_ffn_w2, L0_ffn_shared_gate_up, L0_ffn_shared_down, L0_ffn_shared_gate_w):

    def _L0_attn_ref(x, time_decay, time_first, time_mix_k, time_mix_v, time_mix_r, Wk, Wv, Wr, Wo):
        import jax, jax.numpy as jnp
        import numpy as np
        EPS = 0.0001

        def wkv_log_space(w, u, k, v):
            B, T, D = k.shape
            neg_inf = jnp.full((B, D), -jnp.inf, dtype=k.dtype)

            def step(carry, kv_t):
                ln_ap, ln_am, ln_b = carry
                kt, vt = kv_t
                ln_vp = jnp.log(jnp.maximum(vt, 0) + EPS)
                ln_vm = jnp.log(jnp.maximum(-vt, 0) + EPS)
                uk = u + kt
                denom = jnp.logaddexp(uk, ln_b)
                wkv_t = jnp.exp(jnp.logaddexp(uk + ln_vp, ln_ap) - denom) - jnp.exp(jnp.logaddexp(uk + ln_vm, ln_am) - denom)
                ln_ap = jnp.logaddexp(ln_ap - w, kt + ln_vp)
                ln_am = jnp.logaddexp(ln_am - w, kt + ln_vm)
                ln_b = jnp.logaddexp(ln_b - w, kt)
                return ((ln_ap, ln_am, ln_b), wkv_t)
            kT = jnp.swapaxes(k, 0, 1)
            vT = jnp.swapaxes(v, 0, 1)
            _, wkv = jax.lax.scan(step, (neg_inf, neg_inf, neg_inf), (kT, vT))
            return jnp.swapaxes(wkv, 0, 1)
        B, T, D = x.shape
        last_x = jnp.concatenate([jnp.zeros((B, 1, D), x.dtype), x[:, :-1]], axis=1)
        xk = x * time_mix_k + last_x * (1 - time_mix_k)
        xv = x * time_mix_v + last_x * (1 - time_mix_v)
        xr = x * time_mix_r + last_x * (1 - time_mix_r)
        k = jnp.einsum('btd,ed->bte', xk, Wk)
        v = jnp.einsum('btd,ed->bte', xv, Wv)
        r = jnp.einsum('btd,ed->bte', xr, Wr)
        sr = jax.nn.sigmoid(r)
        w = jnp.exp(time_decay)
        wkv = wkv_log_space(w, time_first, k, v)
        rwkv = wkv * sr
        return jnp.einsum('btd,ed->bte', rwkv, Wo)

    def _L0_ffn_ref(x, router_w, w1, w2, shared_gate_up, shared_down, shared_gate_w):
        import jax, jax.numpy as jnp
        import numpy as np
        D = 256
        F = 256
        E = 8
        K = 2
        B, T = (2, 512)

        def _moe_forward(x, router_w, w1, w2, shared_gate_up, shared_down, shared_gate_w):
            b, t, d = x.shape
            xf = x.reshape(-1, d)
            n = xf.shape[0]
            logits = xf @ router_w
            probs = jax.nn.softmax(logits, axis=-1)
            topw, topi = jax.lax.top_k(probs, K)
            combine = jnp.zeros((n, E), dtype=probs.dtype).at[jnp.arange(n)[:, None], topi].add(topw)
            h = jax.nn.silu(jnp.einsum('nd,edf->nef', xf, w1))
            ye = jnp.einsum('nef,efd->ned', h, w2)
            routed = jnp.einsum('ne,ned->nd', combine, ye)
            gu = xf @ shared_gate_up
            gate, up = (gu[:, :F], gu[:, F:])
            shared = jax.nn.silu(gate) * up @ shared_down
            shared = jax.nn.sigmoid(xf @ shared_gate_w) * shared
            return (routed + shared).reshape(b, t, d)
        return _moe_forward(x, router_w, w1, w2, shared_gate_up, shared_down, shared_gate_w)
    x = L0_attn_x
    x = x + _layernorm(_L0_attn_ref(_layernorm(x, axis=-1), L0_attn_time_decay, L0_attn_time_first, L0_attn_time_mix_k, L0_attn_time_mix_v, L0_attn_time_mix_r, L0_attn_Wk, L0_attn_Wv, L0_attn_Wr, L0_attn_Wo), axis=-1)
    x = x + _layernorm(_L0_ffn_ref(_layernorm(x, axis=-1), L0_ffn_router_w, L0_ffn_w1, L0_ffn_w2, L0_ffn_shared_gate_up, L0_ffn_shared_down, L0_ffn_shared_gate_w), axis=-1)
    return x

_drawn_inputs = setup_inputs


def setup_inputs(seed=0):
    import zlib

    import numpy as np

    out = dict(_drawn_inputs(seed))
    spreads = {}
    factors = {}
    for name, (base, spread) in spreads.items():
        noise = np.random.default_rng([zlib.crc32(name.encode()), seed]).standard_normal(out[name].shape)
        drawn = base * np.exp(spread * noise) if base else spread * noise
        out[name] = jnp.asarray(drawn.astype(out[name].dtype))
    for name, factor in factors.items():
        out[name] = (out[name] * factor).astype(out[name].dtype)
    return out
```

```python
from contextlib import ExitStack

import concourse.bass as bass
from concourse import mybir

ALU = mybir.AluOpType
ACT = mybir.ActivationFunctionType
AX_X = mybir.AxisListType.X
F32 = mybir.dt.float32
F32R = mybir.dt.float32r
U32 = mybir.dt.uint32

P = 128
TC = 512
NT = TC // P
EPS = 1e-5
EMAX = 40.0
PIECE = 1024
CARRY = 4
EULER = 2.718281828459045


class Chunk:

    def __init__(self, base, off):
        self.base, self.off = base, off

    def nth(self, per, k):
        return self.base * per + (self.off * per + k)

    def back(self, n):
        return Chunk(self.base, self.off - n)

    @property
    def first(self):
        return not isinstance(self.base, int) or self.off > 0

    def has(self, n):
        return not isinstance(self.base, int) or self.off >= n

    @property
    def index(self):
        return self.base + self.off


def rwkv_moe(nc, x, decay, u_in, mix_k, mix_v, mix_r, wkT, wvT, wrT, woT, router, w1, w2,
             gate_up, down, gate_w, out):
    B, T, D = x.shape
    E = w1.shape[0]
    H = D // P
    NCH = B * T // TC
    assert D == 256 and E == 8 and T == CARRY * TC and NCH % CARRY == 0
    SLOTS = E + 1
    RW = E + 2

    x_v = x.rearrange("b (c j p) d -> (b c) p j d", j=NT, p=P)
    out_v = out.rearrange("b (c j p) d -> (b c) p j d", j=NT, p=P)

    with ExitStack() as ctx:
        def sb(name, shape, dt=F32):
            return ctx.enter_context(nc.sbuf_tensor(name, shape, dt))

        def sem(name):
            return ctx.enter_context(nc.semaphore(name))

        WP = 12
        wh = sb("wh", [P, WP * PIECE], F32R)
        wl = sb("wl", [P, WP * PIECE], F32R)
        xin = sb("xin", [P, NT, D])
        nrm = sb("nrm", [P, NT * D])
        hT = sb("hT", [P, H, TC + 1])
        dif = sb("dif", [P, H, TC])
        mxh = sb("mxh", [P, H, TC], F32R)
        mxl = sb("mxl", [P, H, TC], F32R)
        kk = sb("kk", [P, H, TC])
        vv = sb("vv", [P, H, TC])
        tr = sb("tr", [P, H, TC])
        st = sb("st", [P, 3, H, TC + 1])
        be = sb("be", [P, H, TC])
        ee = sb("ee", [P, H, TC])
        x1 = sb("x1", [P, 2, NT, D])
        h2h = sb("h2h", [P, H, TC], F32R)
        h2l = sb("h2l", [P, H, TC], F32R)
        hf = sb("hf", [P, 2, TC])
        hh = sb("hh", [P, 2, 2, TC], F32R)
        hl = sb("hl", [P, 2, 2, TC], F32R)
        acc = sb("acc", [P, NT, D])
        fin = sb("fin", [P, NT, D])
        ident = sb("ident", [P, P])
        vec = sb("vec", [P, 5, H])
        negw = sb("negw", [P, H])
        lim = sb("lim", [P, H])
        rwf = sb("rwf", [P, H, RW])
        rwh = sb("rwh", [P, H, RW], F32R)
        rwl = sb("rwl", [P, H, RW], F32R)
        iota8 = sb("iota8", [P, NT, E])
        euler = sb("euler", [P, NT, E])
        mhalf = sb("mhalf", [P, NT])
        zero = sb("zero", [P, H])
        bst = sb("bst", [P, 4, NT, 6])
        mv = sb("mv", [P, 4, NT, 2])
        var = sb("var", [P, 4, NT])
        rstd = sb("rstd", [P, 4, NT])
        lg = sb("lg", [P, NT, RW])
        top = sb("top", [P, NT, 8])
        idx = sb("idx", [P, NT, 8], U32)
        idf = sb("idf", [P, NT, 8])
        ex = sb("ex", [P, NT, E])
        pw = sb("pw", [P, NT, E])
        ssum = sb("ssum", [P, NT])
        m1 = sb("m1", [P, NT, E])
        m2 = sb("m2", [P, NT, E])
        sgt = sb("sgt", [P, NT])
        cw = sb("cw", [P, NT, SLOTS])

        PA = [ctx.enter_context(nc.psum_tensor(f"PA{i}", [P, TC], F32)) for i in range(4)]
        Z = [ctx.enter_context(nc.psum_tensor(f"Z{i}", [P, TC], F32)) for i in range(2)]
        Y = [ctx.enter_context(nc.psum_tensor(f"Y{i}", [P, TC], F32)) for i in range(2)]

        nrm_r = nrm[:, :].rearrange("p (j d) -> p j d", j=NT)
        nrm_c = nrm[:, :].rearrange("p (a t) -> p a t", a=H)

        def view(t, piece, off, n):
            a = piece * PIECE + off
            return t[:, a:a + H * n].rearrange("p (a n) -> p a n", a=H)

        def both(piece, off, n):
            return view(wh, piece, off, n), view(wl, piece, off, n)

        Wk, Wv, Wr, Wo = (both(i // 2, (i % 2) * H * D, D) for i in range(4))
        W1 = [both(2 + e // 2, (e % 2) * H * D, D) for e in range(E)]
        W2 = [both(6 + e // 2, (e % 2) * H * D, D) for e in range(E)]
        Wg = both(10, 0, 2 * D)
        Wd = both(11, 0, D)
        MH = (mxh, mxl)
        stage = [kk, vv, tr, be]

        def src_mat(m):
            return m.rearrange("(a p) n -> p a n", p=P)

        loads = [[(0, src_mat(wkT)), (H * D, src_mat(wvT))], [(0, src_mat(wrT)), (H * D, src_mat(woT))]]
        for w in (w1, w2):
            for e in range(0, E, 2):
                loads.append([(0, src_mat(w[e])), (H * D, src_mat(w[e + 1]))])
        loads.append([(0, src_mat(gate_up))])
        loads.append([(0, src_mat(down))])

        s_const = sem("s_const")
        s_held = [sem("s_held_pool"), sem("s_held_dve")]
        s_vec = sem("s_vec")
        s_prep = sem("s_prep")
        s_aprep = sem("s_aprep")
        s_wld = [sem(f"s_wld{i}") for i in range(4)]
        s_wh = sem("s_wh")
        s_wl = sem("s_wl")
        s_x = sem("s_x")
        s_bst = [sem(f"s_bst{i}") for i in range(4)]
        s_mv = [sem(f"s_mv{i}") for i in range(4)]
        s_rstd = [sem(f"s_rstd{i}") for i in range(4)]
        s_nx = sem("s_nx")
        s_T1 = sem("s_T1")
        s_hT = sem("s_hT")
        s_dif = sem("s_dif")
        s_mix = sem("s_mix")
        s_mxh = sem("s_mxh")
        s_mxl = sem("s_mxl")
        s_proj = sem("s_proj")
        s_kvr = sem("s_kvr")
        s_carry = sem("s_carry")
        s_P = sem("s_P")
        s_dP = sem("s_dP")
        s_al = sem("s_al")
        s_kP = sem("s_kP")
        s_be = sem("s_be")
        s_lag = sem("s_lag")
        s_E = sem("s_E")
        s_bv = sem("s_bv")
        s_scan = sem("s_scan")
        s_ev = sem("s_ev")
        s_num = sem("s_num")
        s_den = sem("s_den")
        s_rec = sem("s_rec")
        s_gt = sem("s_gt")
        s_rw = sem("s_rw")
        s_rwh = sem("s_rwh")
        s_rwl = sem("s_rwl")
        s_O = sem("s_O")
        s_on = sem("s_on")
        s_x1 = sem("s_x1")
        s_h2 = sem("s_h2")
        s_T2 = sem("s_T2")
        s_h2h = sem("s_h2h")
        s_h2l = sem("s_h2l")
        s_rt = sem("s_rt")
        s_lg = sem("s_lg")
        s_route = sem("s_route")
        s_pw = sem("s_pw")
        s_sg = sem("s_sg")
        s_z = sem("s_z")
        s_hs = sem("s_hs")
        s_hu = sem("s_hu")
        s_hh = sem("s_hh")
        s_hl = sem("s_hl")
        s_y = sem("s_y")
        s_acc = sem("s_acc")
        s_fin = sem("s_fin")
        s_fo = sem("s_fo")
        s_out = sem("s_out")

        NROUTE = 10

        LOOP = NCH - CARRY

        def program(eng, body, tail):
            body(Chunk(0, 0), None)
            body(Chunk(0, 1), Chunk(0, 0))
            with eng.Fori(0, LOOP // CARRY) as i:
                for q in range(CARRY):
                    body(Chunk(i * CARRY, 2 + q), Chunk(i * CARRY, 1 + q))
            for c in range(LOOP + 2, NCH):
                body(Chunk(0, c), Chunk(0, c - 1))
            tail(Chunk(0, NCH - 1))

        block = ctx.enter_context(nc.Block())

        @block.sync
        def _(sp):
            with nc.allow_non_contiguous_dma(reason="small vectors, once"):
                for i, v in enumerate((mix_k, mix_v, mix_r)):
                    sp.dma_start(vec[:, i, :], v.rearrange("o t (a p) -> p (o t a)", p=P)).then_inc(s_vec, 16)
                for i, v in enumerate((u_in, decay)):
                    sp.dma_start(vec[:, 3 + i, :], v.rearrange("(a p) -> p a", p=P)).then_inc(s_vec, 16)
                sp.wait_ge(s_const, 3)
                sp.dma_start(rwf[:, :, 0:E], src_mat(router)).then_inc(s_vec, 16)
                sp.dma_start(rwf[:, :, E:E + 1], src_mat(gate_w)).then_inc(s_vec, 16)
            for n, parts in enumerate(loads):
                if n >= 4:
                    sp.wait_ge(s_wh, n - 3)
                    sp.wait_ge(s_wl, n - 3)
                for off, src in parts:
                    w = src.shape[2]
                    dst = stage[n % 4][:, :, :].rearrange("p a t -> p (a t)")[:, off:off + H * w]
                    sp.dma_start(dst.rearrange("p (a n) -> p a n", a=H), src).then_inc(s_wld[n % 4], 16)
                if n == 1:
                    sp.dma_start(xin[:, :, :], x_v[0]).then_inc(s_x, 16)

            def body(c, m):
                sp.wait_ge(s_x1, c.nth(1, 1))
                last = isinstance(c.base, int) and c.off == NCH - 1
                if not last:
                    sp.dma_start(xin[:, :, :], x_v[c.base + (c.off + 1)]).then_inc(s_x, 16)
                if m is not None:
                    store(m)

            def store(m):
                sp.wait_ge(s_fo, m.nth(1, 1))
                sp.dma_start(out_v[m.index], fin[:, :, :]).then_inc(s_out, 16)

            program(sp, body, store)
            sp.wait_ge(s_out, 16 * NCH)

        @block.gpsimd
        def _(pool):
            nc.gpsimd.memset(ident[:, :], 0.0).then_inc(s_const, 1)
            pool.wait_ge(s_const, 1)
            nc.gpsimd.affine_select(out=ident[:, :], in_=ident[:, :], compare_op=ALU.not_equal, fill=1.0,
                                    base=0, pattern=[[-1, P]], channel_multiplier=1).then_inc(s_const, 1)
            nc.gpsimd.memset(rwf[:, :, :], 0.0).then_inc(s_const, 1)
            nc.gpsimd.memset(euler[:, :, :], EULER).then_inc(s_const, 1)
            nc.gpsimd.memset(mhalf[:, :], -0.5).then_inc(s_const, 1)
            nc.gpsimd.memset(zero[:, :], 0.0).then_inc(s_const, 1)
            for e in range(E):
                nc.gpsimd.memset(iota8[:, :, e:e + 1], float(e)).then_inc(s_const, 1)
            pool.wait_ge(s_const, 6 + E)
            pool.wait_ge(s_prep, 2)

            def norm_scale(n, c):
                pool.wait_ge(s_mv[n], c.nth(NT, NT))
                pool.sem_inc(s_held[0], 1)
                nc.gpsimd.tensor_scalar(var[:, n, :], mv[:, n, :, 1], EPS, None, ALU.add).then_inc(s_rstd[n], 1)
                pool.wait_ge(s_rstd[n], c.nth(2, 1))
                nc.gpsimd.tensor_tensor(rstd[:, n, :], var[:, n, :], mhalf[:, :], ALU.pow).then_inc(s_rstd[n], 1)

            def attention(c):
                norm_scale(0, c)
                pool.wait_ge(s_hT, c.nth(3, 3))
                if c.has(1):
                    pool.wait_ge(s_scan, c.back(1).nth(4, 4))
                nc.gpsimd.tensor_tensor(dif[:, :, :], hT[:, :, 1:TC + 1], hT[:, :, 0:TC],
                                        ALU.subtract).then_inc(s_dif, 1)
                pool.wait_ge(s_P, c.nth(2, 2))
                pool.wait_ge(s_mix, c.nth(6, 6))
                nc.gpsimd.tensor_tensor(dif[:, :, :], st[:, 0, :, 1:TC + 1], st[:, 0, :, 0:TC],
                                        ALU.subtract).then_inc(s_dP, 1)
                if c.has(1):
                    pool.wait_ge(s_rw, c.back(1).nth(1, 1))
                nc.gpsimd.tensor_tensor(ee[:, :, :], kk[:, :, :], st[:, 0, :, 0:TC],
                                        ALU.subtract).then_inc(s_lag, 1)
                pool.wait_ge(s_lag, c.nth(3, 1))
                pool.sem_inc(s_held[0], 1)
                for a in range(H):
                    nc.gpsimd.tensor_scalar(ee[:, a, :], ee[:, a, :], lim[:, a:a + 1], None,
                                            ALU.min).then_inc(s_lag, 1)
                pool.wait_ge(s_ev, c.nth(1, 1))
                pool.wait_ge(s_scan, c.nth(4, 4))
                nc.gpsimd.tensor_tensor(ee[:, :, :], ee[:, :, :], st[:, 1, :, 0:TC], ALU.add).then_inc(s_den, 1)
                nc.gpsimd.tensor_tensor(vv[:, :, :], vv[:, :, :], st[:, 2, :, 0:TC], ALU.add).then_inc(s_num, 1)
                norm_scale(1, c)
                pool.wait_ge(s_on, c.nth(NT, NT))
                nc.gpsimd.tensor_tensor(x1[:, c.off % 2, :, :], x1[:, c.off % 2, :, :], xin[:, :, :],
                                        ALU.add).then_inc(s_x1, 1)
                norm_scale(2, c)

            def route(c):
                pool.wait_ge(s_route, c.nth(NROUTE, 2))
                nc.gpsimd.tensor_tensor(pw[:, :, :], euler[:, :, :], ex[:, :, :], ALU.pow).then_inc(s_pw, 1)

            def final(m):
                norm_scale(3, m)
                pool.wait_ge(s_fin, m.nth(NT, NT))
                pool.wait_ge(s_x1, m.nth(1, 1))
                nc.gpsimd.tensor_tensor(fin[:, :, :], fin[:, :, :], x1[:, m.off % 2, :, :],
                                        ALU.add).then_inc(s_fo, 1)

            def body(c, m):
                attention(c)
                if m is not None:
                    final(m)
                route(c)

            program(pool, body, final)

        @block.scalar
        def _(act):
            copy = nc.scalar.copy
            act.wait_ge(s_vec, 16 * 7)
            nc.scalar.activation(negw[:, :], vec[:, 4, :], ACT.Exp).then_inc(s_aprep, 1)
            copy(rwh[:, :, :], rwf[:, :, :]).then_inc(s_aprep, 1)
            filled = [0] * 4
            for n, parts in enumerate(loads):
                filled[n % 4] += 16 * len(parts)
                act.wait_ge(s_wld[n % 4], filled[n % 4])
                w = sum(H * src.shape[2] for _, src in parts)
                flat = stage[n % 4][:, :, :].rearrange("p a t -> p (a t)")
                copy(wh[:, n * PIECE:n * PIECE + w], flat[:, 0:w]).then_inc(s_wh, 1)
            act.wait_ge(s_const, 6 + E)
            act.wait_ge(s_prep, 3)
            act.wait_ge(s_wl, WP)

            def transposed(c):
                if c.has(1):
                    act.wait_ge(s_mix, c.back(1).nth(6, 6))
                start = c.off % CARRY == 0
                if start:
                    copy(hT[:, :, 0], zero[:, :]).then_inc(s_hT, 1)
                else:
                    copy(hT[:, :, 0], hT[:, :, TC]).then_inc(s_hT, 1)
                act.wait_ge(s_hT, c.nth(3, 1))
                for a in range(H):
                    act.wait_ge(s_T1, c.nth(2, a + 1))
                    copy(hT[:, a, 1:TC + 1], PA[a][:, :]).then_inc(s_hT, 1)

            def mix_high(c, i):
                act.wait_ge(s_mix, c.nth(6, 2 * i + 2))
                if i:
                    act.wait_ge(s_proj, c.nth(6, 2 * i))
                elif c.has(1):
                    act.wait_ge(s_O, c.back(1).nth(2, 2))
                copy(mxh[:, :, :], nrm_c).then_inc(s_mxh, 1)

            def evacuate(c, i):
                if c.has(1):
                    act.wait_ge(s_gt, c.back(1).nth(1, 1))
                for a in range(H):
                    act.wait_ge(s_proj, c.nth(6, 2 * i + a + 1))
                    src = PA[(2 + 2 * i + a) % 4]
                    if i < 2:
                        copy((kk, vv)[i][:, a, :], src[:, :]).then_inc(s_kvr, 1)
                    else:
                        nc.scalar.activation(tr[:, a, :], src[:, :], ACT.Tanh, scale=0.5).then_inc(s_kvr, 1)

            def exps(c):
                act.wait_ge(s_kP, c.nth(1, 1))
                nc.scalar.activation(be[:, :, :], be[:, :, :], ACT.Exp).then_inc(s_be, 1)
                act.wait_ge(s_dP, c.nth(1, 1))
                for a in range(H):
                    nc.scalar.activation(dif[:, a, :], dif[:, a, :], ACT.Exp, scale=-1.0,
                                         bias=negw[:, a:a + 1]).then_inc(s_al, 1)
                act.wait_ge(s_lag, c.nth(3, 3))
                for a in range(H):
                    nc.scalar.activation(ee[:, a, :], ee[:, a, :], ACT.Exp, scale=1.0,
                                         bias=vec[:, 3, a:a + 1]).then_inc(s_E, 1)

            def rw_high(c):
                act.wait_ge(s_rw, c.nth(1, 1))
                act.wait_ge(s_proj, c.nth(6, 6))
                copy(mxh[:, :, :], nrm_c).then_inc(s_rwh, 1)

            def h2_high(c):
                for a in range(H):
                    act.wait_ge(s_T2, c.nth(2, a + 1))
                    copy(h2h[:, a, :], PA[2 + a][:, :]).then_inc(s_h2h, 1)

            def gate(c):
                act.wait_ge(s_lg, c.nth(1, 1))
                nc.scalar.activation(sgt[:, :], lg[:, :, E], ACT.Tanh, scale=0.5).then_inc(s_sg, 1)

            def silu(m, s):
                for f in range(2):
                    act.wait_ge(s_z, m.nth(2 * (E + 2), 2 * s + f + 1))
                    if s:
                        act.wait_ge(s_hl, m.nth(2 * SLOTS, 2 * (s - 1) + f + 1))
                    elif m.has(1):
                        act.wait_ge(s_hl, m.back(1).nth(2 * SLOTS, 2 * E + f + 1))
                    nc.scalar.activation(hf[:, f, :], Z[f][:, :], ACT.Silu).then_inc(s_hs, 1)
                    if s < E:
                        high(m, s, f)

            def high(m, s, f):
                if s < E:
                    act.wait_ge(s_hs, m.nth(2 * SLOTS, 2 * s + f + 1))
                else:
                    act.wait_ge(s_hu, m.nth(2, f + 1))
                if s >= 2:
                    act.wait_ge(s_y, m.nth(2 * SLOTS, 2 * (s - 2) + 2))
                elif m.has(1):
                    act.wait_ge(s_y, m.back(1).nth(2 * SLOTS, 2 * (SLOTS - 1 - s % 2) + 2))
                copy(hh[:, s % 2, f, :], hf[:, f, :]).then_inc(s_hh, 1)

            def body(c, m):
                def part(s):
                    if m is not None:
                        silu(m, s)
                part(0)
                transposed(c)
                part(1)
                mix_high(c, 0)
                mix_high(c, 1)
                part(2)
                evacuate(c, 0)
                mix_high(c, 2)
                part(3)
                evacuate(c, 1)
                evacuate(c, 2)
                exps(c)
                part(4)
                part(5)
                part(6)
                rw_high(c)
                part(7)
                part(8)
                if m is not None:
                    for f in range(2):
                        high(m, E, f)
                h2_high(c)
                gate(c)

            def tail(m):
                for s in range(E + 1):
                    silu(m, s)
                for f in range(2):
                    high(m, E, f)

            program(act, body, tail)

        @block.vector
        def _(dve):
            V = nc.vector
            dve.wait_ge(s_vec, 16 * 7)
            dve.wait_ge(s_aprep, 2)
            V.tensor_scalar(negw[:, :], negw[:, :], -1.0, None, ALU.mult).then_inc(s_prep, 1)
            V.tensor_scalar(lim[:, :], vec[:, 3, :], -1.0, EMAX, ALU.mult, ALU.add).then_inc(s_prep, 1)
            V.tensor_tensor(rwl[:, :, :], rwf[:, :, :], rwh[:, :, :].bitcast(F32), ALU.subtract).then_inc(s_prep, 1)
            for n, parts in enumerate(loads):
                dve.wait_ge(s_wh, n + 1)
                w = sum(H * src.shape[2] for _, src in parts)
                flat = stage[n % 4][:, :, :].rearrange("p a t -> p (a t)")
                V.tensor_tensor(wl[:, n * PIECE:n * PIECE + w], flat[:, 0:w],
                                wh[:, n * PIECE:n * PIECE + w].bitcast(F32), ALU.subtract).then_inc(s_wl, 1)
            dve.wait_ge(s_prep, 3)
            dve.wait_ge(s_wl, WP)
            dve.wait_ge(s_const, 6 + E)

            def stats(n, c, tile):
                for j in range(NT):
                    V.bn_stats(bst[:, n, j, :], tile(j)).then_inc(s_bst[n], 1)
                dve.wait_ge(s_bst[n], c.nth(NT, NT))
                dve.sem_inc(s_held[1], 1)
                for j in range(NT):
                    V.bn_aggr(mv[:, n, j, :], bst[:, n, j, :]).then_inc(s_mv[n], 1)

            def normed(n, c, out_tile, tile, done):
                dve.wait_ge(s_rstd[n], c.nth(2, 2))
                for j in range(NT):
                    V.tensor_scalar(out_tile(j), tile(j), mv[:, n, j, 0:1], rstd[:, n, j:j + 1],
                                    ALU.subtract, ALU.mult).then_inc(done, 1)

            def norm_x(c):
                dve.wait_ge(s_x, c.nth(16, 16))
                stats(0, c, lambda j: xin[:, j, :])
                if c.has(1):
                    dve.wait_ge(s_T2, c.back(1).nth(2, 2))
                normed(0, c, lambda j: nrm_r[:, j, :], lambda j: xin[:, j, :], s_nx)

            def mix(c, i):
                if i == 0:
                    dve.wait_ge(s_dif, c.nth(1, 1))
                    dve.wait_ge(s_T1, c.nth(2, 2))
                else:
                    dve.wait_ge(s_mxh, c.nth(3, i))
                    dve.wait_ge(s_mxl, c.nth(3, i))
                for a in range(H):
                    V.scalar_tensor_tensor(out=nrm_c[:, a, :], in0=dif[:, a, :], scalar=vec[:, i, a:a + 1],
                                           in1=hT[:, a, 0:TC], op0=ALU.mult, op1=ALU.add).then_inc(s_mix, 1)
                dve.wait_ge(s_mxh, c.nth(3, i + 1))
                V.tensor_tensor(mxl[:, :, :], nrm_c, mxh[:, :, :].bitcast(F32), ALU.subtract).then_inc(s_mxl, 1)

            def running_max(c):
                start = c.off % CARRY == 0
                if c.has(1):
                    dve.wait_ge(s_den, c.back(1).nth(1, 1))
                    dve.wait_ge(s_num, c.back(1).nth(1, 1))
                if start:
                    V.memset(st[:, 0, :, 0:1], -1e30).then_inc(s_carry, 1)
                    V.memset(st[:, 1:3, :, 0:1], 0.0).then_inc(s_carry, 1)
                else:
                    V.tensor_copy(st[:, 0, :, 0:1], st[:, 0, :, TC:TC + 1]).then_inc(s_carry, 1)
                    V.tensor_copy(st[:, 1:3, :, 0:1], st[:, 1:3, :, TC:TC + 1]).then_inc(s_carry, 1)
                dve.wait_ge(s_carry, c.nth(2, 2))
                for a in range(H):
                    dve.wait_ge(s_kvr, c.nth(6, a + 1))
                    V.tensor_tensor_scan(st[:, 0, a, 1:TC + 1], negw[:, a:a + 1].to_broadcast([P, TC]),
                                         kk[:, a, :], st[:, 0, a, 0:1], ALU.add, ALU.max).then_inc(s_P, 1)
                dve.wait_ge(s_P, c.nth(2, 2))
                V.tensor_tensor(be[:, :, :], kk[:, :, :], st[:, 0, :, 1:TC + 1], ALU.subtract).then_inc(s_kP, 1)

            def scans(c):
                dve.wait_ge(s_be, c.nth(1, 1))
                dve.wait_ge(s_kvr, c.nth(6, 4))
                dve.wait_ge(s_lag, c.nth(3, 1))
                V.tensor_tensor(kk[:, :, :], be[:, :, :], vv[:, :, :], ALU.mult).then_inc(s_bv, 1)
                for a in range(H):
                    dve.wait_ge(s_al, c.nth(2, a + 1))
                    V.tensor_tensor_scan(st[:, 1, a, 1:TC + 1], dif[:, a, :], be[:, a, :], st[:, 1, a, 0:1],
                                         ALU.mult, ALU.add).then_inc(s_scan, 1)
                dve.wait_ge(s_bv, c.nth(1, 1))
                for a in range(H):
                    V.tensor_tensor_scan(st[:, 2, a, 1:TC + 1], dif[:, a, :], kk[:, a, :], st[:, 2, a, 0:1],
                                         ALU.mult, ALU.add).then_inc(s_scan, 1)
                dve.wait_ge(s_E, c.nth(2, 2))
                V.tensor_tensor(vv[:, :, :], ee[:, :, :], vv[:, :, :], ALU.mult).then_inc(s_ev, 1)

            def reciprocals(c):
                dve.wait_ge(s_den, c.nth(1, 1))
                V.reciprocal(ee[:, :, :], ee[:, :, :]).then_inc(s_rec, 1)

            def receptance(c):
                dve.wait_ge(s_num, c.nth(1, 1))
                dve.wait_ge(s_kvr, c.nth(6, 6))
                V.scalar_tensor_tensor(out=vv[:, :, :], in0=tr[:, :, :], scalar=1.0, in1=vv[:, :, :],
                                       op0=ALU.add, op1=ALU.mult).then_inc(s_gt, 1)
                dve.wait_ge(s_rec, c.nth(1, 1))
                dve.wait_ge(s_gt, c.nth(1, 1))
                V.scalar_tensor_tensor(out=nrm_c, in0=vv[:, :, :], scalar=0.5, in1=ee[:, :, :],
                                       op0=ALU.mult, op1=ALU.mult).then_inc(s_rw, 1)
                dve.wait_ge(s_rwh, c.nth(1, 1))
                V.tensor_tensor(mxl[:, :, :], nrm_c, mxh[:, :, :].bitcast(F32), ALU.subtract).then_inc(s_rwl, 1)

            def norm_out(c):
                def tile(j):
                    return PA[j // 2][:, (j % 2) * D:(j % 2 + 1) * D]
                dve.wait_ge(s_O, c.nth(2, 2))
                stats(1, c, tile)
                if c.has(2):
                    dve.wait_ge(s_fo, c.back(2).nth(1, 1))
                normed(1, c, lambda j: x1[:, c.off % 2, j, :], tile, s_on)

            def norm_h2(c):
                dve.wait_ge(s_x1, c.nth(1, 1))
                stats(2, c, lambda j: x1[:, c.off % 2, j, :])
                dve.wait_ge(s_rwh, c.nth(1, 1))
                dve.wait_ge(s_rwl, c.nth(1, 1))
                normed(2, c, lambda j: nrm_r[:, j, :], lambda j: x1[:, c.off % 2, j, :], s_h2)

            def h2_low(c):
                for a in range(H):
                    dve.wait_ge(s_h2h, c.nth(2, a + 1))
                    V.tensor_tensor(h2l[:, a, :], PA[2 + a][:, :], h2h[:, a, :].bitcast(F32),
                                    ALU.subtract).then_inc(s_h2l, 1)

            def route(c):
                step = [0]

                def done(ins):
                    step[0] += 1
                    ins.then_inc(s_route, 1)

                def after(k):
                    dve.wait_ge(s_route, c.nth(NROUTE, k))

                dve.wait_ge(s_rt, c.nth(1, 1))
                V.tensor_copy(lg[:, :, :], PA[0][:, 0:NT * RW].rearrange("p (j e) -> p j e", j=NT)
                              ).then_inc(s_lg, 1)
                dve.wait_ge(s_lg, c.nth(1, 1))
                dve.sem_inc(s_held[1], 1)
                for j in range(NT):
                    last = V.max(top[:, j, :], lg[:, j, 0:E])
                done(last)
                after(1)
                done(V.tensor_tensor(ex[:, :, :], lg[:, :, 0:E], top[:, :, 0:1].to_broadcast([P, NT, E]),
                                     ALU.subtract))
                for j in range(NT):
                    last = V.max_index(idx[:, j, :], top[:, j, :], lg[:, j, 0:E])
                done(last)
                after(3)
                done(V.tensor_copy(idf[:, :, :], idx[:, :, :]))
                after(4)
                V.tensor_tensor(m1[:, :, :], iota8[:, :, :], idf[:, :, 0:1].to_broadcast([P, NT, E]), ALU.is_equal)
                done(V.tensor_tensor(m2[:, :, :], iota8[:, :, :], idf[:, :, 1:2].to_broadcast([P, NT, E]),
                                     ALU.is_equal))
                after(5)
                done(V.tensor_tensor(m1[:, :, :], m1[:, :, :], m2[:, :, :], ALU.add))
                dve.wait_ge(s_pw, c.nth(1, 1))
                done(V.tensor_reduce(ssum[:, :], pw[:, :, :], AX_X, ALU.add))
                after(7)
                V.reciprocal(ssum[:, :], ssum[:, :])
                done(V.tensor_tensor(m2[:, :, :], m1[:, :, :], pw[:, :, :], ALU.mult))
                after(8)
                done(V.tensor_tensor(cw[:, :, 0:E], m2[:, :, :],
                                     ssum[:, :].unsqueeze(2).to_broadcast([P, NT, E]), ALU.mult))
                dve.wait_ge(s_sg, c.nth(1, 1))
                done(V.tensor_scalar(cw[:, :, E], sgt[:, :], 0.5, 0.5, ALU.mult, ALU.add))
                assert step[0] == NROUTE

            def low(m, s):
                for f in range(2):
                    dve.wait_ge(s_hh, m.nth(2 * SLOTS, 2 * s + f + 1))
                    V.tensor_tensor(hl[:, s % 2, f, :], hf[:, f, :], hh[:, s % 2, f, :].bitcast(F32),
                                    ALU.subtract).then_inc(s_hl, 1)

            def shared_hidden(m):
                for f in range(2):
                    dve.wait_ge(s_hs, m.nth(2 * SLOTS, 2 * E + f + 1))
                    dve.wait_ge(s_z, m.nth(2 * (E + 2), 2 * (E + 1) + f + 1))
                    V.tensor_tensor(hf[:, f, :], hf[:, f, :], Z[f][:, :], ALU.mult).then_inc(s_hu, 1)

            def gather(m, s):
                if s == 0:
                    dve.wait_ge(s_route, m.nth(NROUTE, NROUTE))
                    if m.has(1):
                        dve.wait_ge(s_fin, m.back(1).nth(NT, NT))
                for j in range(NT):
                    if j % 2 == 0:
                        dve.wait_ge(s_y, m.nth(2 * SLOTS, 2 * s + j // 2 + 1))
                    y = Y[j // 2][:, (j % 2) * D:(j % 2 + 1) * D]
                    if s == 0:
                        V.tensor_scalar(acc[:, j, :], y, cw[:, j, 0:1], None, ALU.mult).then_inc(s_acc, 1)
                    else:
                        dve.wait_ge(s_acc, m.nth(NT * SLOTS, NT * (s - 1) + j + 1))
                        V.scalar_tensor_tensor(out=acc[:, j, :], in0=y, scalar=cw[:, j, s:s + 1],
                                               in1=acc[:, j, :], op0=ALU.mult, op1=ALU.add).then_inc(s_acc, 1)

            def final(m):
                dve.wait_ge(s_acc, m.nth(NT * SLOTS, NT * SLOTS))
                stats(3, m, lambda j: acc[:, j, :])
                if m.has(1):
                    dve.wait_ge(s_out, m.back(1).nth(16, 16))
                normed(3, m, lambda j: fin[:, j, :], lambda j: acc[:, j, :], s_fin)

            def body(c, m):
                def part(f, s):
                    if m is not None:
                        f(m, s)
                norm_x(c)
                part(low, 0)
                part(low, 1)
                mix(c, 0)
                part(gather, 0)
                mix(c, 1)
                part(low, 2)
                part(gather, 1)
                mix(c, 2)
                part(low, 3)
                part(gather, 2)
                running_max(c)
                part(low, 4)
                part(gather, 3)
                scans(c)
                part(low, 5)
                part(gather, 4)
                reciprocals(c)
                part(low, 6)
                part(gather, 5)
                receptance(c)
                part(low, 7)
                part(gather, 6)
                if m is not None:
                    shared_hidden(m)
                part(low, 8)
                part(gather, 7)
                norm_out(c)
                norm_h2(c)
                part(gather, 8)
                h2_low(c)
                if m is not None:
                    final(m)
                route(c)

            def tail(m):
                for s in range(E):
                    low(m, s)
                    if s:
                        gather(m, s - 1)
                shared_hidden(m)
                low(m, E)
                gather(m, E - 1)
                gather(m, E)
                final(m)

            program(dve, body, tail)

        @block.tensor
        def _(pe):
            mm = nc.tensor.matmul

            def product(out_ap, terms, first=True, last=True):
                todo = []
                for (lh, ll), (rh, rl) in terms:
                    todo += [(lh, rh), (lh, rl), (ll, rh)]
                for n, (l, r) in enumerate(todo):
                    ins = mm(out_ap, l, r, start=(n == 0), stop=(n == len(todo) - 1))
                return ins

            def transposes(c, banks, done):
                for a in range(H):
                    for j in range(NT):
                        ins = nc.tensor.transpose(PA[banks + a][:, j * P:(j + 1) * P],
                                                  nrm_r[:, j, a * P:(a + 1) * P], ident[:, :])
                    ins.then_inc(done, 1)

            def T1(c):
                pe.wait_ge(s_nx, c.nth(NT, NT))
                if c.has(1):
                    pe.wait_ge(s_lg, c.back(1).nth(1, 1))
                transposes(c, 0, s_T1)

            def proj(c, i):
                pe.wait_ge(s_mxh, c.nth(3, i + 1))
                pe.wait_ge(s_mxl, c.nth(3, i + 1))
                if i == 0:
                    if c.has(1):
                        pe.wait_ge(s_h2l, c.back(1).nth(2, 2))
                elif i == 1:
                    pe.wait_ge(s_hT, c.nth(3, 3))
                else:
                    pe.wait_ge(s_kvr, c.nth(6, 2))
                W = (Wk, Wv, Wr)[i]
                for e in range(H):
                    product(PA[(2 + 2 * i + e) % 4][:, :],
                            [((W[0][:, a, e * P:(e + 1) * P], W[1][:, a, e * P:(e + 1) * P]),
                              (mxh[:, a, :], mxl[:, a, :])) for a in range(H)]).then_inc(s_proj, 1)

            def out_product(c):
                pe.wait_ge(s_rwh, c.nth(1, 1))
                pe.wait_ge(s_rwl, c.nth(1, 1))
                pe.wait_ge(s_kvr, c.nth(6, 4))
                for j in range(NT):
                    ins = product(PA[j // 2][:, (j % 2) * D:(j % 2 + 1) * D],
                                  [((mxh[:, a, j * P:(j + 1) * P], mxl[:, a, j * P:(j + 1) * P]),
                                    (Wo[0][:, a, :], Wo[1][:, a, :])) for a in range(H)])
                    if j % 2:
                        ins.then_inc(s_O, 1)

            def T2(c):
                pe.wait_ge(s_h2, c.nth(NT, NT))
                pe.wait_ge(s_kvr, c.nth(6, 6))
                transposes(c, 2, s_T2)

            def router_product(c):
                pe.wait_ge(s_h2l, c.nth(2, 2))
                pe.wait_ge(s_on, c.nth(NT, NT))
                for j in range(NT):
                    ins = product(PA[0][:, j * RW:(j + 1) * RW],
                                  [((h2h[:, a, j * P:(j + 1) * P], h2l[:, a, j * P:(j + 1) * P]),
                                    (rwh[:, a, :], rwl[:, a, :])) for a in range(H)])
                ins.then_inc(s_rt, 1)

            def hidden(m, s):
                W, off = (W1[s], 0) if s < E else (Wg, (s - E) * D)
                if s == 0:
                    pe.wait_ge(s_h2l, m.nth(2, 2))
                for f in range(2):
                    if s:
                        pe.wait_ge(s_hs, m.nth(2 * SLOTS, 2 * (s - 1) + f + 1))
                    elif m.has(1):
                        pe.wait_ge(s_hu, m.back(1).nth(2, f + 1))
                    cols = slice(off + f * P, off + (f + 1) * P)
                    product(Z[f][:, :], [((W[0][:, a, cols], W[1][:, a, cols]), (h2h[:, a, :], h2l[:, a, :]))
                                         for a in range(H)]).then_inc(s_z, 1)

            def outputs(m, s):
                W = W2[s] if s < E else Wd
                pe.wait_ge(s_hl, m.nth(2 * SLOTS, 2 * s + 2))
                for j in range(NT):
                    if j % 2 == 0:
                        if s:
                            pe.wait_ge(s_acc, m.nth(NT * SLOTS, NT * (s - 1) + j + 2))
                        elif m.has(1):
                            pe.wait_ge(s_acc, m.back(1).nth(NT * SLOTS, NT * E + j + 2))
                    ins = product(Y[j // 2][:, (j % 2) * D:(j % 2 + 1) * D],
                                  [((hh[:, s % 2, f, j * P:(j + 1) * P], hl[:, s % 2, f, j * P:(j + 1) * P]),
                                    (W[0][:, f, :], W[1][:, f, :])) for f in range(2)])
                    if j % 2:
                        ins.then_inc(s_y, 1)

            pe.wait_ge(s_const, 6 + E)
            pe.wait_ge(s_prep, 3)
            pe.wait_ge(s_wl, WP)

            def body(c, m):
                def part(f, s):
                    if m is not None:
                        f(m, s)
                part(hidden, 0)
                T1(c)
                part(hidden, 1)
                part(outputs, 0)
                proj(c, 0)
                part(hidden, 2)
                part(outputs, 1)
                proj(c, 1)
                part(hidden, 3)
                part(outputs, 2)
                proj(c, 2)
                part(hidden, 4)
                part(outputs, 3)
                part(hidden, 5)
                part(outputs, 4)
                part(hidden, 6)
                part(outputs, 5)
                part(hidden, 7)
                part(outputs, 6)
                out_product(c)
                part(hidden, 8)
                part(outputs, 7)
                part(hidden, 9)
                T2(c)
                part(outputs, 8)
                router_product(c)

            def tail(m):
                for s in range(E + 2):
                    hidden(m, s)
                    if s and s <= E:
                        outputs(m, s - 1)
                outputs(m, E)

            program(pe, body, tail)


_VECTORS = ["L0_attn_time_decay", "L0_attn_time_first", "L0_attn_time_mix_k", "L0_attn_time_mix_v",
            "L0_attn_time_mix_r"]
_TURNED = ["L0_attn_Wk", "L0_attn_Wv", "L0_attn_Wr", "L0_attn_Wo"]
_FFN = ["L0_ffn_router_w", "L0_ffn_w1", "L0_ffn_w2", "L0_ffn_shared_gate_up", "L0_ffn_shared_down",
        "L0_ffn_shared_gate_w"]


def kernel(**inputs):
    import numpy as _np
    import concourse.bacc as _bacc
    from concourse import mybir as _mybir
    from concourse.bass_utils import run_bass_kernel_spmd as _run

    nc = _bacc.Bacc("TRN2", target_bir_lowering=False, num_devices=1)
    arrays, args = {}, []
    for name in ["L0_attn_x"] + _VECTORS + _TURNED + _FFN:
        a = _np.asarray(inputs[name])
        a = _np.ascontiguousarray(a.T if name in _TURNED else a)
        arrays[f"in_{name}"] = a
        args.append(nc.dram_tensor(f"in_{name}", a.shape, _mybir.dt.from_np(a.dtype), kind="ExternalInput").ap())
    shape = arrays["in_L0_attn_x"].shape
    out = nc.dram_tensor("out", shape, _mybir.dt.float32, kind="ExternalOutput").ap()
    rwkv_moe(nc, *args, out)
    r = _run(nc, [arrays], core_ids=[0])
    return r.results[0]["out"]
```

```python
from contextlib import ExitStack

import concourse.bass as bass
from concourse import mybir

ALU = mybir.AluOpType
ACT = mybir.ActivationFunctionType
AX_X = mybir.AxisListType.X
F32 = mybir.dt.float32
F32R = mybir.dt.float32r
U32 = mybir.dt.uint32

P = 128
TC = 512
NT = TC // P
EPS = 1e-5
EBOUND = 2.0 ** 57
PIECE = 1024
CARRY = 4


class Chunk:

    def __init__(self, base, off):
        self.base, self.off = base, off

    def nth(self, per, k):
        return self.base * per + (self.off * per + k)

    def pair(self, per, k):
        return self.base * (per // 2) + (self.off // 2 * per + k)

    def ahead(self, n):
        return Chunk(self.base, self.off + n)

    def back(self, n):
        return Chunk(self.base, self.off - n)

    def has(self, n):
        return not isinstance(self.base, int) or self.off >= n

    @property
    def index(self):
        return self.base + self.off


def rwkv_moe(nc, x, decay, u_in, mix_k, mix_v, mix_r, wkT, wvT, wrT, woT, router, w1, w2,
             gate_up, down, gate_w, out):
    B, T, D = x.shape
    E = w1.shape[0]
    H = D // P
    NCH = B * T // TC
    assert D == 256 and E == 8 and T == CARRY * TC and NCH % CARRY == 0
    SLOTS = E + 1
    RW = E + 2

    x_v = x.rearrange("b (c j p) d -> (b c) p j d", j=NT, p=P)
    out_v = out.rearrange("b (c j p) d -> (b c) p j d", j=NT, p=P)

    with ExitStack() as ctx:
        def sb(name, shape, dt=F32):
            return ctx.enter_context(nc.sbuf_tensor(name, shape, dt))

        def sem(name):
            return ctx.enter_context(nc.semaphore(name))

        WP = 12
        wh = sb("wh", [P, WP * PIECE - H * D], F32R)
        wl = sb("wl", [P, WP * PIECE - H * D], F32R)
        xin = sb("xin", [P, 2, NT, D])
        nx = sb("nx", [P, NT, D])
        nrm = sb("nrm", [P, NT * D])
        hT = sb("hT", [P, H, TC + 1])
        dif = sb("dif", [P, H, TC])
        mxh = sb("mxh", [P, H, TC], F32R)
        mxl = sb("mxl", [P, H, TC], F32R)
        kk = sb("kk", [P, H, TC])
        vv = sb("vv", [P, H, TC])
        tr = sb("tr", [P, H, TC])
        st = sb("st", [P, 3, H, TC + 1])
        be = sb("be", [P, H, TC])
        ee = sb("ee", [P, H, TC])
        x1 = sb("x1", [P, 2, NT, D])
        h2h = sb("h2h", [P, H, TC], F32R)
        h2l = sb("h2l", [P, H, TC], F32R)
        hf = sb("hf", [P, 2, TC])
        hh = sb("hh", [P, 2, 2, TC], F32R)
        hl = sb("hl", [P, 2, 2, TC], F32R)
        acc = sb("acc", [P, NT, D])
        ysc = sb("ysc", [P, 2, 2, D])
        fin = sb("fin", [P, NT, D])
        ident = sb("ident", [P, P])
        vec = sb("vec", [P, 5, H])
        negw = sb("negw", [P, H])
        rwf = sb("rwf", [P, H, RW])
        rwh = sb("rwh", [P, H, RW], F32R)
        rwl = sb("rwl", [P, H, RW], F32R)
        iota8 = sb("iota8", [P, NT, E])
        mhalf = sb("mhalf", [P, NT])
        zero = sb("zero", [P, H])
        bst = sb("bst", [P, 4, NT, 6])
        mv = sb("mv", [P, 4, NT, 2])
        var = sb("var", [P, 4, NT])
        rstd = sb("rstd", [P, 4, NT])
        lg = sb("lg", [P, NT, RW])
        top = sb("top", [P, NT, 8])
        idx = sb("idx", [P, NT, 8], U32)
        idf = sb("idf", [P, NT, 8])
        ex = sb("ex", [P, NT, E])
        pw = sb("pw", [P, NT, E])
        ssum = sb("ssum", [P, NT])
        m1 = sb("m1", [P, NT, E])
        m2 = sb("m2", [P, NT, E])
        sgt = sb("sgt", [P, NT])
        cw = sb("cw", [P, NT, SLOTS])

        PA = [ctx.enter_context(nc.psum_tensor(f"PA{i}", [P, TC], F32)) for i in range(4)]
        Z = [ctx.enter_context(nc.psum_tensor(f"Z{i}", [P, TC], F32)) for i in range(2)]
        Y = [ctx.enter_context(nc.psum_tensor(f"Y{i}", [P, TC], F32)) for i in range(2)]

        nrm_r = nrm[:, :].rearrange("p (j d) -> p j d", j=NT)
        nrm_c = nrm[:, :].rearrange("p (a t) -> p a t", a=H)

        def view(t, piece, off, n):
            a = piece * PIECE + off
            return t[:, a:a + H * n].rearrange("p (a n) -> p a n", a=H)

        def both(piece, off, n):
            return view(wh, piece, off, n), view(wl, piece, off, n)

        Wk, Wv, Wr, Wo = (both(i // 2, (i % 2) * H * D, D) for i in range(4))
        W1 = [both(2 + e // 2, (e % 2) * H * D, D) for e in range(E)]
        W2 = [both(6 + e // 2, (e % 2) * H * D, D) for e in range(E)]
        Wg = both(10, 0, 2 * D)
        Wd = both(11, 0, D)
        MH = (mxh, mxl)
        stage = [kk, vv, tr, be]

        def src_mat(m):
            return m.rearrange("(a p) n -> p a n", p=P)

        loads = [[(0, src_mat(wkT)), (H * D, src_mat(wvT))], [(0, src_mat(wrT)), (H * D, src_mat(woT))]]
        for w in (w1, w2):
            for e in range(0, E, 2):
                loads.append([(0, src_mat(w[e])), (H * D, src_mat(w[e + 1]))])
        loads.append([(0, src_mat(gate_up))])
        loads.append([(0, src_mat(down))])

        s_const = sem("s_const")
        s_held = [sem("s_held_pool"), sem("s_held_dve")]
        s_vec = sem("s_vec")
        s_prep = sem("s_prep")
        s_aprep = sem("s_aprep")
        s_wld = [sem(f"s_wld{i}") for i in range(4)]
        s_wh = sem("s_wh")
        s_wl = sem("s_wl")
        s_x = [sem("s_x0"), sem("s_x1in")]
        s_bst = [sem(f"s_bst{i}") for i in range(4)]
        s_mv = [sem(f"s_mv{i}") for i in range(4)]
        s_rstd = [sem(f"s_rstd{i}") for i in range(4)]
        s_nx = sem("s_nx")
        s_T1 = sem("s_T1")
        s_hT = sem("s_hT")
        s_dif = sem("s_dif")
        s_mix = sem("s_mix")
        s_mxh = sem("s_mxh")
        s_mxl = sem("s_mxl")
        s_proj = sem("s_proj")
        s_kvr = sem("s_kvr")
        s_carry = sem("s_carry")
        s_P = sem("s_P")
        s_dP = sem("s_dP")
        s_al = sem("s_al")
        s_kP = sem("s_kP")
        s_be = sem("s_be")
        s_lag = sem("s_lag")
        s_E = sem("s_E")
        s_bv = sem("s_bv")
        s_scan = sem("s_scan")
        s_ev = sem("s_ev")
        s_num = sem("s_num")
        s_den = sem("s_den")
        s_rec = sem("s_rec")
        s_gt = sem("s_gt")
        s_rw = sem("s_rw")
        s_rwh = sem("s_rwh")
        s_rwl = sem("s_rwl")
        s_O = sem("s_O")
        s_on = sem("s_on")
        s_x1 = sem("s_x1")
        s_h2 = sem("s_h2")
        s_T2 = sem("s_T2")
        s_h2h = sem("s_h2h")
        s_h2l = sem("s_h2l")
        s_rt = sem("s_rt")
        s_lg = sem("s_lg")
        s_route = sem("s_route")
        s_pw = sem("s_pw")
        s_sg = sem("s_sg")
        s_z = sem("s_z")
        s_hs = sem("s_hs")
        s_hu = sem("s_hu")
        s_hh = sem("s_hh")
        s_hl = sem("s_hl")
        s_y = sem("s_y")
        s_acc = sem("s_acc")
        s_ysc = sem("s_ysc")
        s_ac2 = sem("s_ac2")
        s_fin = sem("s_fin")
        s_fo = sem("s_fo")
        s_out = sem("s_out")

        NROUTE = 10

        LOOP = NCH - CARRY

        def program(eng, body, tail, front=None):
            if front is not None:
                front(Chunk(0, 0))
            body(Chunk(0, 0), None)
            body(Chunk(0, 1), Chunk(0, 0))
            with eng.Fori(0, LOOP // CARRY) as i:
                for q in range(CARRY):
                    body(Chunk(i * CARRY, 2 + q), Chunk(i * CARRY, 1 + q))
            for c in range(LOOP + 2, NCH):
                body(Chunk(0, c), Chunk(0, c - 1))
            tail(Chunk(0, NCH - 1))

        def follows(c, n):
            return not isinstance(c.base, int) or c.off + n < NCH

        block = ctx.enter_context(nc.Block())

        @block.sync
        def _(sp):
            with nc.allow_non_contiguous_dma(reason="small vectors, once"):
                for i, v in enumerate((mix_k, mix_v, mix_r)):
                    sp.dma_start(vec[:, i, :], v.rearrange("o t (a p) -> p (o t a)", p=P)).then_inc(s_vec, 16)
                for i, v in enumerate((u_in, decay)):
                    sp.dma_start(vec[:, 3 + i, :], v.rearrange("(a p) -> p a", p=P)).then_inc(s_vec, 16)
                sp.wait_ge(s_const, 3)
                sp.dma_start(rwf[:, :, 0:E], src_mat(router)).then_inc(s_vec, 16)
                sp.dma_start(rwf[:, :, E:E + 1], src_mat(gate_w)).then_inc(s_vec, 16)
            for n, parts in enumerate(loads):
                if n >= 4:
                    sp.wait_ge(s_wh, n - 3)
                    sp.wait_ge(s_wl, n - 3)
                for off, src in parts:
                    w = src.shape[2]
                    dst = stage[n % 4][:, :, :].rearrange("p a t -> p (a t)")[:, off:off + H * w]
                    sp.dma_start(dst.rearrange("p (a n) -> p a n", a=H), src).then_inc(s_wld[n % 4], 16)
                if n < 2:
                    sp.dma_start(xin[:, n, :, :], x_v[n]).then_inc(s_x[n], 16)

            def body(c, m):
                if m is not None and m.has(1):
                    store(m.back(1))
                sp.wait_ge(s_x1, c.nth(1, 1))
                if follows(c, 2):
                    sp.dma_start(xin[:, c.off % 2, :, :], x_v[c.ahead(2).index]).then_inc(s_x[c.off % 2], 16)

            def store(m):
                sp.wait_ge(s_fo, m.nth(1, 1))
                sp.dma_start(out_v[m.index], fin[:, :, :]).then_inc(s_out, 16)

            def tail(m):
                store(m.back(1))
                store(m)

            program(sp, body, tail)
            sp.wait_ge(s_out, 16 * NCH)

        @block.gpsimd
        def _(pool):
            nc.gpsimd.memset(ident[:, :], 0.0).then_inc(s_const, 1)
            pool.wait_ge(s_const, 1)
            nc.gpsimd.affine_select(out=ident[:, :], in_=ident[:, :], compare_op=ALU.not_equal, fill=1.0,
                                    base=0, pattern=[[-1, P]], channel_multiplier=1).then_inc(s_const, 1)
            nc.gpsimd.memset(rwf[:, :, :], 0.0).then_inc(s_const, 1)
            nc.gpsimd.memset(mhalf[:, :], -0.5).then_inc(s_const, 1)
            nc.gpsimd.memset(zero[:, :], 0.0).then_inc(s_const, 1)
            for e in range(E):
                nc.gpsimd.memset(iota8[:, :, e:e + 1], float(e)).then_inc(s_const, 1)
            pool.wait_ge(s_const, 5 + E)

            def norm_scale(n, c):
                pool.wait_ge(s_mv[n], c.nth(NT, NT))
                pool.sem_inc(s_held[0], 1)
                nc.gpsimd.tensor_scalar(var[:, n, :], mv[:, n, :, 1], EPS, None, ALU.add).then_inc(s_rstd[n], 1)
                pool.wait_ge(s_rstd[n], c.nth(2, 1))
                nc.gpsimd.tensor_tensor(rstd[:, n, :], var[:, n, :], mhalf[:, :], ALU.pow).then_inc(s_rstd[n], 1)

            def mix_low(c, i):
                pool.wait_ge(s_mxh, c.nth(3, i + 1))
                if i:
                    pool.wait_ge(s_proj, c.nth(6, 2 * i))
                elif c.has(1):
                    pool.wait_ge(s_O, c.back(1).nth(2, 2))
                nc.gpsimd.tensor_tensor(mxl[:, :, :], nrm_c, mxh[:, :, :].bitcast(F32),
                                        ALU.subtract).then_inc(s_mxl, 1)

            def front(c):
                pool.wait_ge(s_hT, c.nth(3, 3))
                if c.has(1):
                    pool.wait_ge(s_scan, c.back(1).nth(4, 4))
                nc.gpsimd.tensor_tensor(dif[:, :, :], hT[:, :, 1:TC + 1], hT[:, :, 0:TC],
                                        ALU.subtract).then_inc(s_dif, 1)
                mix_low(c, 0)

            def add(m, s):
                if m is not None:
                    pool.wait_ge(s_ysc, m.nth(2 * SLOTS, 2 * s + 2))
                    if s > 1:
                        pool.wait_ge(s_ac2, m.nth(E, s - 1))
                    nc.gpsimd.tensor_tensor(acc[:, 2:4, :], acc[:, 2:4, :], ysc[:, s % 2, :, :],
                                            ALU.add).then_inc(s_ac2, 1)

            def attention(c, m):
                mix_low(c, 1)
                if m is not None and m.has(1):
                    final(m.back(1))
                mix_low(c, 2)
                add(m, 1)
                pool.wait_ge(s_P, c.nth(2, 2))
                pool.wait_ge(s_mix, c.nth(6, 6))
                nc.gpsimd.tensor_tensor(dif[:, :, :], st[:, 0, :, 1:TC + 1], st[:, 0, :, 0:TC],
                                        ALU.subtract).then_inc(s_dP, 1)
                if c.has(1):
                    pool.wait_ge(s_rw, c.back(1).nth(1, 1))
                first = int(c.off % CARRY == 0)
                if first:
                    pool.sem_inc(s_held[0], 1)
                    nc.gpsimd.memset(ee[:, :, 0:1], 0.0).then_inc(s_lag, 1)
                nc.gpsimd.tensor_tensor(ee[:, :, first:TC], kk[:, :, first:TC], st[:, 0, :, first:TC],
                                        ALU.subtract).then_inc(s_lag, 2 - first)
                add(m, 2)
                add(m, 3)
                pool.wait_ge(s_ev, c.nth(1, 1))
                pool.wait_ge(s_scan, c.nth(4, 4))
                nc.gpsimd.tensor_tensor(vv[:, :, :], vv[:, :, :], st[:, 2, :, 0:TC], ALU.add).then_inc(s_num, 1)
                for s in (4, 5, 6):
                    add(m, s)
                norm_scale(1, c)
                if follows(c, 1):
                    norm_scale(0, c.ahead(1))
                pool.wait_ge(s_on, c.nth(NT, NT))
                nc.gpsimd.tensor_tensor(x1[:, c.off % 2, :, :], x1[:, c.off % 2, :, :], xin[:, c.off % 2, :, :],
                                        ALU.add).then_inc(s_x1, 1)
                norm_scale(2, c)

            def final(m):
                norm_scale(3, m)
                pool.wait_ge(s_fin, m.nth(NT, NT))
                pool.wait_ge(s_x1, m.nth(1, 1))
                nc.gpsimd.tensor_tensor(fin[:, :, :], fin[:, :, :], x1[:, m.off % 2, :, :],
                                        ALU.add).then_inc(s_fo, 1)

            def body(c, m):
                attention(c, m)
                add(m, 7)
                if follows(c, 1):
                    front(c.ahead(1))
                add(m, 8)

            def tail(m):
                final(m.back(1))
                for s in range(1, SLOTS):
                    add(m, s)
                final(m)

            def begin(c):
                norm_scale(0, c)
                front(c)

            program(pool, body, tail, begin)

        @block.scalar
        def _(act):
            copy = nc.scalar.copy
            act.wait_ge(s_vec, 16 * 7)
            nc.scalar.activation(negw[:, :], vec[:, 4, :], ACT.Exp).then_inc(s_aprep, 1)
            copy(rwh[:, :, :], rwf[:, :, :]).then_inc(s_aprep, 1)
            filled = [0] * 4
            for n, parts in enumerate(loads):
                filled[n % 4] += 16 * len(parts)
                act.wait_ge(s_wld[n % 4], filled[n % 4])
                w = sum(H * src.shape[2] for _, src in parts)
                flat = stage[n % 4][:, :, :].rearrange("p a t -> p (a t)")
                copy(wh[:, n * PIECE:n * PIECE + w], flat[:, 0:w]).then_inc(s_wh, 1)
            act.wait_ge(s_const, 5 + E)
            act.wait_ge(s_prep, 2)
            act.wait_ge(s_wl, WP)

            def transposed(c):
                if c.has(1):
                    act.wait_ge(s_mix, c.back(1).nth(6, 6))
                start = c.off % CARRY == 0
                if start:
                    copy(hT[:, :, 0], zero[:, :]).then_inc(s_hT, 1)
                else:
                    copy(hT[:, :, 0], hT[:, :, TC]).then_inc(s_hT, 1)
                act.wait_ge(s_hT, c.nth(3, 1))
                for a in range(H):
                    act.wait_ge(s_T1, c.nth(2, a + 1))
                    copy(hT[:, a, 1:TC + 1], PA[a][:, :]).then_inc(s_hT, 1)

            def mix_high(c, i):
                act.wait_ge(s_mix, c.nth(6, 2 * i + 2))
                if i:
                    act.wait_ge(s_proj, c.nth(6, 2 * i))
                elif c.has(1):
                    act.wait_ge(s_O, c.back(1).nth(2, 2))
                copy(mxh[:, :, :], nrm_c).then_inc(s_mxh, 1)

            def evacuate(c, i):
                if c.has(1):
                    act.wait_ge(s_gt, c.back(1).nth(1, 1))
                for a in range(H):
                    act.wait_ge(s_proj, c.nth(6, 2 * i + a + 1))
                    src = PA[(2 + 2 * i + a) % 4]
                    if i < 2:
                        copy((kk, vv)[i][:, a, :], src[:, :]).then_inc(s_kvr, 1)
                    else:
                        nc.scalar.activation(tr[:, a, :], src[:, :], ACT.Tanh, scale=0.5).then_inc(s_kvr, 1)

            def exps(c):
                act.wait_ge(s_kP, c.nth(1, 1))
                nc.scalar.activation(be[:, :, :], be[:, :, :], ACT.Exp).then_inc(s_be, 1)
                act.wait_ge(s_dP, c.nth(1, 1))
                for a in range(H):
                    nc.scalar.activation(dif[:, a, :], dif[:, a, :], ACT.Exp, scale=-1.0,
                                         bias=negw[:, a:a + 1]).then_inc(s_al, 1)
                act.wait_ge(s_lag, c.nth(2, 2))
                for a in range(H):
                    nc.scalar.activation(ee[:, a, :], ee[:, a, :], ACT.Exp, scale=1.0,
                                         bias=vec[:, 3, a:a + 1]).then_inc(s_E, 1)

            def rw_high(c):
                act.wait_ge(s_rw, c.nth(1, 1))
                act.wait_ge(s_proj, c.nth(6, 6))
                copy(mxh[:, :, :], nrm_c).then_inc(s_rwh, 1)

            def h2_high(c):
                for a in range(H):
                    act.wait_ge(s_T2, c.nth(2, a + 1))
                    copy(h2h[:, a, :], PA[2 + a][:, :]).then_inc(s_h2h, 1)

            def gate(c):
                act.wait_ge(s_route, c.nth(NROUTE, 2))
                nc.scalar.activation(pw[:, :, :], ex[:, :, :], ACT.Exp).then_inc(s_pw, 1)
                nc.scalar.activation(sgt[:, :], lg[:, :, E], ACT.Tanh, scale=0.5).then_inc(s_sg, 1)

            def silu(m, s):
                for f in range(2):
                    act.wait_ge(s_z, m.nth(2 * (E + 2), 2 * s + f + 1))
                    if s:
                        act.wait_ge(s_hl, m.nth(2 * SLOTS, 2 * (s - 1) + f + 1))
                    elif m.has(1):
                        act.wait_ge(s_hl, m.back(1).nth(2 * SLOTS, 2 * E + f + 1))
                    nc.scalar.activation(hf[:, f, :], Z[f][:, :], ACT.Silu).then_inc(s_hs, 1)
                    if s < E:
                        high(m, s, f)

            def high(m, s, f):
                if s < E:
                    act.wait_ge(s_hs, m.nth(2 * SLOTS, 2 * s + f + 1))
                else:
                    act.wait_ge(s_hu, m.nth(2, f + 1))
                if s >= 2:
                    act.wait_ge(s_y, m.nth(2 * SLOTS, 2 * (s - 2) + 2))
                elif m.has(1):
                    act.wait_ge(s_y, m.back(1).nth(2 * SLOTS, 2 * (SLOTS - 1 - s % 2) + 2))
                copy(hh[:, s % 2, f, :], hf[:, f, :]).then_inc(s_hh, 1)

            def weigh(m, s):
                act.wait_ge(s_y, m.nth(2 * SLOTS, 2 * s + 2))
                if s == 0:
                    act.wait_ge(s_route, m.nth(NROUTE, NROUTE))
                    if m.has(1):
                        act.wait_ge(s_fin, m.back(1).nth(NT, NT))
                elif s >= 3:
                    act.wait_ge(s_ac2, m.nth(E, s - 2))
                elif m.has(1):
                    act.wait_ge(s_ac2, m.back(1).nth(E, E))
                for j in (2, 3):
                    to = ysc[:, s % 2, j - 2, :] if s else acc[:, j, :]
                    nc.scalar.activation(to, Y[1][:, (j % 2) * D:(j % 2 + 1) * D], ACT.Copy,
                                         scale=cw[:, j, s:s + 1]).then_inc(s_ysc, 1)

            def body(c, m):
                def part(s):
                    if m is not None:
                        silu(m, s)

                def weighed(s):
                    if m is not None:
                        weigh(m, s)
                part(0)
                mix_high(c, 1)
                if m is not None:
                    gate(m)
                part(1)
                part(2)
                evacuate(c, 0)
                weighed(0)
                mix_high(c, 2)
                part(3)
                evacuate(c, 1)
                weighed(1)
                weighed(2)
                evacuate(c, 2)
                exps(c)
                for s in range(4, 7):
                    part(s)
                    weighed(s - 1)
                rw_high(c)
                part(7)
                weighed(6)
                part(8)
                if follows(c, 1):
                    transposed(c.ahead(1))
                weighed(7)
                if m is not None:
                    for f in range(2):
                        high(m, E, f)
                h2_high(c)
                weighed(8)
                if follows(c, 1):
                    mix_high(c.ahead(1), 0)

            def begin(c):
                transposed(c)
                mix_high(c, 0)

            def tail(m):
                silu(m, 0)
                gate(m)
                for s in range(1, E + 1):
                    silu(m, s)
                    weigh(m, s - 1)
                for f in range(2):
                    high(m, E, f)
                weigh(m, E)

            program(act, body, tail, begin)

        @block.vector
        def _(dve):
            V = nc.vector
            dve.wait_ge(s_vec, 16 * 7)
            dve.wait_ge(s_aprep, 2)
            V.tensor_scalar(negw[:, :], negw[:, :], -1.0, None, ALU.mult).then_inc(s_prep, 1)
            V.tensor_tensor(rwl[:, :, :], rwf[:, :, :], rwh[:, :, :].bitcast(F32), ALU.subtract).then_inc(s_prep, 1)
            for n, parts in enumerate(loads):
                dve.wait_ge(s_wh, n + 1)
                w = sum(H * src.shape[2] for _, src in parts)
                flat = stage[n % 4][:, :, :].rearrange("p a t -> p (a t)")
                V.tensor_tensor(wl[:, n * PIECE:n * PIECE + w], flat[:, 0:w],
                                wh[:, n * PIECE:n * PIECE + w].bitcast(F32), ALU.subtract).then_inc(s_wl, 1)
            dve.wait_ge(s_prep, 2)
            dve.wait_ge(s_wl, WP)
            dve.wait_ge(s_const, 5 + E)

            def stats(n, c, tile):
                for j in range(NT):
                    V.bn_stats(bst[:, n, j, :], tile(j)).then_inc(s_bst[n], 1)
                dve.wait_ge(s_bst[n], c.nth(NT, NT))
                dve.sem_inc(s_held[1], 1)
                for j in range(NT):
                    V.bn_aggr(mv[:, n, j, :], bst[:, n, j, :]).then_inc(s_mv[n], 1)

            def normed(n, c, out_tile, tile, done):
                dve.wait_ge(s_rstd[n], c.nth(2, 2))
                for j in range(NT):
                    V.tensor_scalar(out_tile(j), tile(j), mv[:, n, j, 0:1], rstd[:, n, j:j + 1],
                                    ALU.subtract, ALU.mult).then_inc(done, 1)

            def stats_x(c):
                dve.wait_ge(s_x[c.off % 2], c.pair(16, 16))
                stats(0, c, lambda j: xin[:, c.off % 2, j, :])

            def norm_x(c):
                if c.has(1):
                    dve.wait_ge(s_T1, c.back(1).nth(2, 2))
                normed(0, c, lambda j: nx[:, j, :], lambda j: xin[:, c.off % 2, j, :], s_nx)

            def mix(c, i):
                if i == 0:
                    dve.wait_ge(s_dif, c.nth(1, 1))
                    if c.has(1):
                        dve.wait_ge(s_T2, c.back(1).nth(2, 2))
                else:
                    dve.wait_ge(s_mxh, c.nth(3, i))
                    dve.wait_ge(s_mxl, c.nth(3, i))
                for a in range(H):
                    V.scalar_tensor_tensor(out=nrm_c[:, a, :], in0=dif[:, a, :], scalar=vec[:, i, a:a + 1],
                                           in1=hT[:, a, 0:TC], op0=ALU.mult, op1=ALU.add).then_inc(s_mix, 1)

            def running_max(c):
                start = c.off % CARRY == 0
                if c.has(1):
                    dve.wait_ge(s_den, c.back(1).nth(1, 1))
                    dve.wait_ge(s_num, c.back(1).nth(1, 1))
                if start:
                    V.memset(st[:, 0, :, 0:1], -1e30).then_inc(s_carry, 1)
                    V.memset(st[:, 1:3, :, 0:1], 0.0).then_inc(s_carry, 1)
                else:
                    V.tensor_copy(st[:, 0, :, 0:1], st[:, 0, :, TC:TC + 1]).then_inc(s_carry, 1)
                    V.tensor_copy(st[:, 1:3, :, 0:1], st[:, 1:3, :, TC:TC + 1]).then_inc(s_carry, 1)
                dve.wait_ge(s_carry, c.nth(2, 2))
                for a in range(H):
                    dve.wait_ge(s_kvr, c.nth(6, a + 1))
                    V.tensor_tensor_scan(st[:, 0, a, 1:TC + 1], negw[:, a:a + 1].to_broadcast([P, TC]),
                                         kk[:, a, :], st[:, 0, a, 0:1], ALU.add, ALU.max).then_inc(s_P, 1)
                dve.wait_ge(s_P, c.nth(2, 2))
                V.tensor_tensor(be[:, :, :], kk[:, :, :], st[:, 0, :, 1:TC + 1], ALU.subtract).then_inc(s_kP, 1)

            def scans(c):
                dve.wait_ge(s_be, c.nth(1, 1))
                dve.wait_ge(s_kvr, c.nth(6, 4))
                dve.wait_ge(s_lag, c.nth(2, 2))
                V.tensor_tensor(kk[:, :, :], be[:, :, :], vv[:, :, :], ALU.mult).then_inc(s_bv, 1)
                for a in range(H):
                    dve.wait_ge(s_al, c.nth(2, a + 1))
                    V.tensor_tensor_scan(st[:, 1, a, 1:TC + 1], dif[:, a, :], be[:, a, :], st[:, 1, a, 0:1],
                                         ALU.mult, ALU.add).then_inc(s_scan, 1)
                dve.wait_ge(s_bv, c.nth(1, 1))
                for a in range(H):
                    V.tensor_tensor_scan(st[:, 2, a, 1:TC + 1], dif[:, a, :], kk[:, a, :], st[:, 2, a, 0:1],
                                         ALU.mult, ALU.add).then_inc(s_scan, 1)
                dve.wait_ge(s_E, c.nth(2, 2))
                V.scalar_tensor_tensor(out=vv[:, :, :], in0=ee[:, :, :], scalar=EBOUND, in1=vv[:, :, :],
                                       op0=ALU.min, op1=ALU.mult).then_inc(s_ev, 1)
                dve.wait_ge(s_ev, c.nth(1, 1))
                dve.wait_ge(s_scan, c.nth(4, 2))
                V.scalar_tensor_tensor(out=ee[:, :, :], in0=ee[:, :, :], scalar=EBOUND, in1=st[:, 1, :, 0:TC],
                                       op0=ALU.min, op1=ALU.add).then_inc(s_den, 1)

            def reciprocals(c, a):
                dve.wait_ge(s_den, c.nth(1, 1))
                V.reciprocal(ee[:, a, :], ee[:, a, :]).then_inc(s_rec, 1)

            def receptance(c):
                dve.wait_ge(s_num, c.nth(1, 1))
                dve.wait_ge(s_kvr, c.nth(6, 6))
                V.scalar_tensor_tensor(out=vv[:, :, :], in0=tr[:, :, :], scalar=1.0, in1=vv[:, :, :],
                                       op0=ALU.add, op1=ALU.mult).then_inc(s_gt, 1)
                dve.wait_ge(s_rec, c.nth(2, 2))
                dve.wait_ge(s_gt, c.nth(1, 1))
                V.scalar_tensor_tensor(out=nrm_c, in0=vv[:, :, :], scalar=0.5, in1=ee[:, :, :],
                                       op0=ALU.mult, op1=ALU.mult).then_inc(s_rw, 1)
                dve.wait_ge(s_rwh, c.nth(1, 1))
                dve.wait_ge(s_proj, c.nth(6, 6))
                V.tensor_tensor(mxl[:, :, :], nrm_c, mxh[:, :, :].bitcast(F32), ALU.subtract).then_inc(s_rwl, 1)

            def norms(c):
                def tile(j):
                    return PA[j // 2][:, (j % 2) * D:(j % 2 + 1) * D]

                def row(j):
                    return x1[:, c.off % 2, j, :]

                dve.wait_ge(s_O, c.nth(2, 2))
                stats(1, c, tile)
                if follows(c, 1):
                    stats_x(c.ahead(1))
                if c.has(2):
                    dve.wait_ge(s_fo, c.back(2).nth(1, 1))
                normed(1, c, row, tile, s_on)
                if follows(c, 1):
                    norm_x(c.ahead(1))
                dve.wait_ge(s_x1, c.nth(1, 1))
                stats(2, c, row)
                dve.wait_ge(s_rwh, c.nth(1, 1))
                dve.wait_ge(s_rwl, c.nth(1, 1))
                normed(2, c, lambda j: nrm_r[:, j, :], row, s_h2)

            def h2_low(c):
                for a in range(H):
                    dve.wait_ge(s_h2h, c.nth(2, a + 1))
                    V.tensor_tensor(h2l[:, a, :], PA[2 + a][:, :], h2h[:, a, :].bitcast(F32),
                                    ALU.subtract).then_inc(s_h2l, 1)

            def logits(c):
                dve.wait_ge(s_rt, c.nth(1, 1))
                V.tensor_copy(lg[:, :, :], PA[0][:, 0:NT * RW].rearrange("p (j e) -> p j e", j=NT)
                              ).then_inc(s_lg, 1)

            def route(c):
                step = [0]

                def done(ins):
                    step[0] += 1
                    ins.then_inc(s_route, 1)

                def after(k):
                    dve.wait_ge(s_route, c.nth(NROUTE, k))

                dve.wait_ge(s_lg, c.nth(1, 1))
                dve.sem_inc(s_held[1], 1)
                for j in range(NT):
                    last = V.max(top[:, j, :], lg[:, j, 0:E])
                done(last)
                after(1)
                done(V.tensor_tensor(ex[:, :, :], lg[:, :, 0:E], top[:, :, 0:1].to_broadcast([P, NT, E]),
                                     ALU.subtract))
                for j in range(NT):
                    last = V.max_index(idx[:, j, :], top[:, j, :], lg[:, j, 0:E])
                done(last)
                after(3)
                done(V.tensor_copy(idf[:, :, :], idx[:, :, :]))
                after(4)
                V.tensor_tensor(m1[:, :, :], iota8[:, :, :], idf[:, :, 0:1].to_broadcast([P, NT, E]), ALU.is_equal)
                done(V.tensor_tensor(m2[:, :, :], iota8[:, :, :], idf[:, :, 1:2].to_broadcast([P, NT, E]),
                                     ALU.is_equal))
                after(5)
                done(V.tensor_tensor(m1[:, :, :], m1[:, :, :], m2[:, :, :], ALU.add))
                dve.wait_ge(s_pw, c.nth(1, 1))
                done(V.tensor_reduce(ssum[:, :], pw[:, :, :], AX_X, ALU.add))
                after(7)
                V.reciprocal(ssum[:, :], ssum[:, :])
                done(V.tensor_tensor(m2[:, :, :], m1[:, :, :], pw[:, :, :], ALU.mult))
                after(8)
                done(V.tensor_tensor(cw[:, :, 0:E], m2[:, :, :],
                                     ssum[:, :].unsqueeze(2).to_broadcast([P, NT, E]), ALU.mult))
                dve.wait_ge(s_sg, c.nth(1, 1))
                done(V.tensor_scalar(cw[:, :, E], sgt[:, :], 0.5, 0.5, ALU.mult, ALU.add))
                assert step[0] == NROUTE

            def low(m, s):
                for f in range(2):
                    dve.wait_ge(s_hh, m.nth(2 * SLOTS, 2 * s + f + 1))
                    V.tensor_tensor(hl[:, s % 2, f, :], hf[:, f, :], hh[:, s % 2, f, :].bitcast(F32),
                                    ALU.subtract).then_inc(s_hl, 1)

            def shared_hidden(m):
                for f in range(2):
                    dve.wait_ge(s_hs, m.nth(2 * SLOTS, 2 * E + f + 1))
                    dve.wait_ge(s_z, m.nth(2 * (E + 2), 2 * (E + 1) + f + 1))
                    V.tensor_tensor(hf[:, f, :], hf[:, f, :], Z[f][:, :], ALU.mult).then_inc(s_hu, 1)

            def gather(m, s):
                if s == 0:
                    dve.wait_ge(s_route, m.nth(NROUTE, NROUTE))
                    if m.has(1):
                        dve.wait_ge(s_fin, m.back(1).nth(NT, NT))
                dve.wait_ge(s_y, m.nth(2 * SLOTS, 2 * s + 1))
                for j in range(2):
                    y = Y[0][:, j * D:(j + 1) * D]
                    if s == 0:
                        V.tensor_scalar(acc[:, j, :], y, cw[:, j, 0:1], None, ALU.mult).then_inc(s_acc, 1)
                    else:
                        dve.wait_ge(s_acc, m.nth(2 * SLOTS, 2 * (s - 1) + j + 1))
                        V.scalar_tensor_tensor(out=acc[:, j, :], in0=y, scalar=cw[:, j, s:s + 1],
                                               in1=acc[:, j, :], op0=ALU.mult, op1=ALU.add).then_inc(s_acc, 1)

            def final_stats(m):
                dve.wait_ge(s_acc, m.nth(2 * SLOTS, 2 * SLOTS))
                dve.wait_ge(s_ac2, m.nth(E, E))
                stats(3, m, lambda j: acc[:, j, :])

            def final(m):
                if m.has(1):
                    dve.wait_ge(s_out, m.back(1).nth(16, 16))
                normed(3, m, lambda j: fin[:, j, :], lambda j: acc[:, j, :], s_fin)

            def body(c, m):
                def part(f, s):
                    if m is not None:
                        f(m, s)
                part(low, 0)
                mix(c, 1)
                if m is not None and m.has(1):
                    final_stats(m.back(1))
                if m is not None:
                    route(m)
                part(low, 1)
                if m is not None and m.has(1):
                    final(m.back(1))
                part(gather, 0)
                mix(c, 2)
                part(low, 2)
                part(gather, 1)
                running_max(c)
                part(low, 3)
                part(gather, 2)
                scans(c)
                part(low, 4)
                part(gather, 3)
                reciprocals(c, 0)
                part(low, 5)
                part(gather, 4)
                reciprocals(c, 1)
                part(low, 6)
                part(gather, 5)
                receptance(c)
                part(low, 7)
                part(gather, 6)
                norms(c)
                part(gather, 7)
                if m is not None:
                    shared_hidden(m)
                part(low, 8)
                h2_low(c)
                if follows(c, 1):
                    mix(c.ahead(1), 0)
                part(gather, 8)
                logits(c)

            def begin(c):
                stats_x(c)
                norm_x(c)
                mix(c, 0)

            def tail(m):
                low(m, 0)
                final_stats(m.back(1))
                route(m)
                final(m.back(1))
                for s in range(1, E):
                    low(m, s)
                    gather(m, s - 1)
                shared_hidden(m)
                low(m, E)
                gather(m, E - 1)
                gather(m, E)
                final_stats(m)
                final(m)

            program(dve, body, tail, begin)

        @block.tensor
        def _(pe):
            mm = nc.tensor.matmul

            def product(out_ap, terms, first=True, last=True):
                todo = []
                for (lh, ll), (rh, rl) in terms:
                    todo += [(lh, rh), (lh, rl), (ll, rh)]
                for n, (l, r) in enumerate(todo):
                    ins = mm(out_ap, l, r, start=(n == 0), stop=(n == len(todo) - 1))
                return ins

            def transposes(rows, banks, done):
                for a in range(H):
                    for j in range(NT):
                        ins = nc.tensor.transpose(PA[banks + a][:, j * P:(j + 1) * P],
                                                  rows[:, j, a * P:(a + 1) * P], ident[:, :])
                    ins.then_inc(done, 1)

            def T1(c):
                pe.wait_ge(s_nx, c.nth(NT, NT))
                if c.has(1):
                    pe.wait_ge(s_on, c.back(1).nth(NT, NT))
                transposes(nx, 0, s_T1)

            def proj(c, i):
                pe.wait_ge(s_mxh, c.nth(3, i + 1))
                pe.wait_ge(s_mxl, c.nth(3, i + 1))
                if i == 0:
                    if c.has(1):
                        pe.wait_ge(s_h2l, c.back(1).nth(2, 2))
                elif i == 1:
                    pe.wait_ge(s_hT, c.nth(3, 3))
                    if c.has(1):
                        pe.wait_ge(s_lg, c.back(1).nth(1, 1))
                else:
                    pe.wait_ge(s_kvr, c.nth(6, 2))
                W = (Wk, Wv, Wr)[i]
                for e in range(H):
                    product(PA[(2 + 2 * i + e) % 4][:, :],
                            [((W[0][:, a, e * P:(e + 1) * P], W[1][:, a, e * P:(e + 1) * P]),
                              (mxh[:, a, :], mxl[:, a, :])) for a in range(H)]).then_inc(s_proj, 1)

            def out_product(c):
                pe.wait_ge(s_rwh, c.nth(1, 1))
                pe.wait_ge(s_rwl, c.nth(1, 1))
                pe.wait_ge(s_kvr, c.nth(6, 4))
                for j in range(NT):
                    ins = product(PA[j // 2][:, (j % 2) * D:(j % 2 + 1) * D],
                                  [((mxh[:, a, j * P:(j + 1) * P], mxl[:, a, j * P:(j + 1) * P]),
                                    (Wo[0][:, a, :], Wo[1][:, a, :])) for a in range(H)])
                    if j % 2:
                        ins.then_inc(s_O, 1)

            def T2(c):
                pe.wait_ge(s_h2, c.nth(NT, NT))
                pe.wait_ge(s_kvr, c.nth(6, 6))
                transposes(nrm_r, 2, s_T2)

            def router_product(c):
                pe.wait_ge(s_h2l, c.nth(2, 2))
                if follows(c, 1):
                    pe.wait_ge(s_hT, c.ahead(1).nth(3, 3))
                else:
                    pe.wait_ge(s_on, c.nth(NT, NT))
                for j in range(NT):
                    ins = product(PA[0][:, j * RW:(j + 1) * RW],
                                  [((h2h[:, a, j * P:(j + 1) * P], h2l[:, a, j * P:(j + 1) * P]),
                                    (rwh[:, a, :], rwl[:, a, :])) for a in range(H)])
                ins.then_inc(s_rt, 1)

            def hidden(m, s):
                W, off = (W1[s], 0) if s < E else (Wg, (s - E) * D)
                if s == 0:
                    pe.wait_ge(s_h2l, m.nth(2, 2))
                for f in range(2):
                    if s:
                        pe.wait_ge(s_hs, m.nth(2 * SLOTS, 2 * (s - 1) + f + 1))
                    elif m.has(1):
                        pe.wait_ge(s_hu, m.back(1).nth(2, f + 1))
                    cols = slice(off + f * P, off + (f + 1) * P)
                    product(Z[f][:, :], [((W[0][:, a, cols], W[1][:, a, cols]), (h2h[:, a, :], h2l[:, a, :]))
                                         for a in range(H)]).then_inc(s_z, 1)

            def outputs(m, s):
                W = W2[s] if s < E else Wd
                pe.wait_ge(s_hl, m.nth(2 * SLOTS, 2 * s + 2))
                for j in range(NT):
                    if j % 2 == 0:
                        bank_read = (s_acc, s_ysc)[j // 2]
                        if s:
                            pe.wait_ge(bank_read, m.nth(2 * SLOTS, 2 * s))
                        elif m.has(1):
                            pe.wait_ge(bank_read, m.back(1).nth(2 * SLOTS, 2 * SLOTS))
                    ins = product(Y[j // 2][:, (j % 2) * D:(j % 2 + 1) * D],
                                  [((hh[:, s % 2, f, j * P:(j + 1) * P], hl[:, s % 2, f, j * P:(j + 1) * P]),
                                    (W[0][:, f, :], W[1][:, f, :])) for f in range(2)])
                    if j % 2:
                        ins.then_inc(s_y, 1)

            pe.wait_ge(s_const, 5 + E)
            pe.wait_ge(s_prep, 2)
            pe.wait_ge(s_wl, WP)

            def body(c, m):
                def part(f, s):
                    if m is not None:
                        f(m, s)
                part(hidden, 0)
                proj(c, 0)
                part(hidden, 1)
                part(outputs, 0)
                part(hidden, 2)
                proj(c, 1)
                part(outputs, 1)
                part(hidden, 3)
                part(outputs, 2)
                proj(c, 2)
                for s in range(4, E):
                    part(hidden, s)
                    part(outputs, s - 1)
                out_product(c)
                part(hidden, 8)
                part(outputs, 7)
                if follows(c, 1):
                    T1(c.ahead(1))
                part(hidden, 9)
                T2(c)
                part(outputs, 8)
                router_product(c)

            def tail(m):
                for s in range(E + 2):
                    hidden(m, s)
                    if s and s <= E:
                        outputs(m, s - 1)
                outputs(m, E)

            program(pe, body, tail, T1)


_VECTORS = ["L0_attn_time_decay", "L0_attn_time_first", "L0_attn_time_mix_k", "L0_attn_time_mix_v",
            "L0_attn_time_mix_r"]
_TURNED = ["L0_attn_Wk", "L0_attn_Wv", "L0_attn_Wr", "L0_attn_Wo"]
_FFN = ["L0_ffn_router_w", "L0_ffn_w1", "L0_ffn_w2", "L0_ffn_shared_gate_up", "L0_ffn_shared_down",
        "L0_ffn_shared_gate_w"]


def kernel(**inputs):
    import numpy as _np
    import concourse.bacc as _bacc
    from concourse import mybir as _mybir
    from concourse.bass_utils import run_bass_kernel_spmd as _run

    nc = _bacc.Bacc("TRN2", target_bir_lowering=False, num_devices=1)
    arrays, args = {}, []
    for name in ["L0_attn_x"] + _VECTORS + _TURNED + _FFN:
        a = _np.asarray(inputs[name])
        a = _np.ascontiguousarray(a.T if name in _TURNED else a)
        arrays[f"in_{name}"] = a
        args.append(nc.dram_tensor(f"in_{name}", a.shape, _mybir.dt.from_np(a.dtype), kind="ExternalInput").ap())
    shape = arrays["in_L0_attn_x"].shape
    out = nc.dram_tensor("out", shape, _mybir.dt.float32, kind="ExternalOutput").ap()
    rwkv_moe(nc, *args, out)
    r = _run(nc, [arrays], core_ids=[0])
    return r.results[0]["out"]
```
